# Optimizing a Trainium2 kernel written in Bass

```python
import numpy as np
import jax
import jax.numpy as jnp

def _softmax(x, axis=-1):
    return jax.nn.softmax(x, axis=axis)

def _gelu(x):
    return jax.nn.gelu(x, approximate=True)

def _silu(x):
    return jax.nn.silu(x)

def _sigmoid(x):
    return jax.nn.sigmoid(x)

def _layernorm(x, axis=-1, eps=1e-05):
    m = jnp.mean(x, axis=axis, keepdims=True)
    v = jnp.var(x, axis=axis, keepdims=True)
    return (x - m) / jnp.sqrt(v + eps)

def _scatter_add(tgt, idx, src, axis=0):
    return tgt.at[idx].add(src)

def _segment_sum(src, seg, n):
    return jax.ops.segment_sum(src, seg, n)
kernel_name = 'mk_gnn_ffn_d2_gnn_r8_8bf2ac'

def setup_inputs(seed: int=0):
    np.random.seed(seed)
    _w = jnp.asarray

    def _rec_inputs():
        import jax
        import jax.numpy as jnp
        _gk = jax.random.key(seed)
        x = -0.0003713 + 1 * jax.random.normal(jax.random.fold_in(_gk, 1), (6250, 256), jnp.float32)
        src = jax.random.randint(jax.random.fold_in(_gk, 2), (100000,), 0, 6250, jnp.int32)
        dst = jax.random.randint(jax.random.fold_in(_gk, 3), (100000,), 0, 6250, jnp.int32)
        _o = jnp.argsort(dst, stable=True)
        src = src[_o]
        dst = dst[_o]
        edge_type_8 = jax.random.randint(jax.random.fold_in(_gk, 13), (100000,), 0, 8, jnp.int32)
        edge_weight = jax.random.uniform(jax.random.fold_in(_gk, 14), (100000,), jnp.float32, 0.0, 1)
        return (x, src, dst, edge_type_8, edge_weight)
    x, src, dst, edge_type_8, edge_weight = _rec_inputs()

    def _L0_gnn_setup():
        import jax, jax.numpy as jnp
        import numpy as np
        N = 6250
        NEG_SLOPE = 0.1

        def gcn_conv(x, edge_index, W, b):
            src, dst = (edge_index[0], edge_index[1])
            loops = jnp.arange(N, dtype=src.dtype)
            row = jnp.concatenate([src, loops])
            col = jnp.concatenate([dst, loops])
            deg = jax.ops.segment_sum(jnp.ones(row.shape, x.dtype), col, num_segments=N)
            dis = jnp.where(deg > 0, jax.lax.rsqrt(deg), 0.0)
            norm = dis[row] * dis[col]
            h = x @ W
            msgs = h[row] * norm[:, None]
            out = jax.ops.segment_sum(msgs, col, num_segments=N)
            return out + b
        key = jax.random.key(seed)
        ks = jax.random.split(key, 9)
        F_in, F = (256, 256)
        E = 100000
        x = jax.random.normal(ks[0], (N, F_in), dtype=jnp.float32)
        edge_index = jax.random.randint(ks[1], (2, E), 0, N, dtype=jnp.int64)
        s_in = 1.0 / np.sqrt(F_in)
        s_f = 1.0 / np.sqrt(F)
        Wp = jax.random.uniform(ks[2], (F_in, F), jnp.float32, -s_in, s_in)
        bp = jax.random.uniform(ks[3], (F,), jnp.float32, -s_in, s_in)
        W1 = jax.random.uniform(ks[4], (F, F), jnp.float32, -s_f, s_f)
        b1 = jax.random.uniform(ks[5], (F,), jnp.float32, -s_f, s_f)
        W2 = jax.random.uniform(ks[6], (F, F), jnp.float32, -s_f, s_f)
        b2 = jax.random.uniform(ks[7], (F,), jnp.float32, -s_f, s_f)
        return {'x': x, 'edge_index': edge_index, 'Wp': Wp, 'bp': bp, 'W1': W1, 'b1': b1, 'W2': W2, 'b2': b2}
    _L0_gnn_all = _L0_gnn_setup()
    _L0_gnn_in = {k: v for k, v in _L0_gnn_all.items() if k in ('Wp', 'bp', 'W1', 'b1', 'W2', 'b2')}
    del _L0_gnn_all

    def _L0_ffn_setup():
        import jax, jax.numpy as jnp
        import numpy as np
        B, T, D, H, E = (16, 512, 256, 512, 8)
        key = jax.random.key(seed)
        ks = jax.random.split(key, 5)
        x = jax.random.normal(ks[0], (B, T, D), dtype=jnp.float32)
        gate_w = jax.random.normal(ks[1], (D, E), dtype=jnp.float32) * 0.02
        gate_b = jnp.zeros((E,), dtype=jnp.float32)
        W1 = jax.random.normal(ks[2], (E, D, H), dtype=jnp.float32) * 0.02
        b1 = jnp.zeros((E, H), dtype=jnp.float32)
        W2 = jax.random.normal(ks[3], (E, H, D), dtype=jnp.float32) * 0.02
        b2 = jnp.zeros((E, D), dtype=jnp.float32)
        return {'x': x, 'gate_w': gate_w, 'gate_b': gate_b, 'W1': W1, 'b1': b1, 'W2': W2, 'b2': b2}
    _L0_ffn_all = _L0_ffn_setup()
    _L0_ffn_in = {k: v for k, v in _L0_ffn_all.items() if k in ('gate_w', 'gate_b', 'W1', 'b1', 'W2', 'b2')}
    del _L0_ffn_all

    def _L1_gnn_setup():
        import jax, jax.numpy as jnp
        import numpy as np
        N_NODES = 5000
        N_EDGES = 80000
        IN_FEAT = 256
        OUT_FEAT = 256
        NUM_RELS = 8
        key = jax.random.key(seed)
        k = jax.random.split(key, 6)
        h = jax.random.normal(k[0], (N_NODES, IN_FEAT), dtype=jnp.float32)
        norm = jax.random.uniform(k[1], (N_EDGES,), dtype=jnp.float32)
        gain = float(np.sqrt(2.0))
        bound = gain * float(np.sqrt(6.0 / (IN_FEAT + OUT_FEAT)))
        weight = jax.random.uniform(k[2], (NUM_RELS, IN_FEAT, OUT_FEAT), dtype=jnp.float32, minval=-bound, maxval=bound)
        edge_src = jax.random.randint(k[3], (N_EDGES,), 0, N_NODES)
        edge_dst = jax.random.randint(k[4], (N_EDGES,), 0, N_NODES)
        edge_type = jax.random.randint(k[5], (N_EDGES,), 0, NUM_RELS)
        return {'h': h, 'norm': norm, 'weight': weight, 'edge_src': edge_src, 'edge_dst': edge_dst, 'edge_type': edge_type}
    _L1_gnn_all = _L1_gnn_setup()
    _L1_gnn_in = {k: v for k, v in _L1_gnn_all.items() if k in ('weight',)}
    del _L1_gnn_all

    def _L1_ffn_setup():
        import jax, jax.numpy as jnp
        import numpy as np
        NUM_EXPERTS = 8
        TOP_K = 2
        B, S, D = (8, 1024, 256)

        def _moe(tokens, router_w, w1, b1, w2, b2):
            N = tokens.shape[0]
            E = router_w.shape[0]
            logits = tokens.astype(jnp.float32) @ router_w.astype(jnp.float32).T
            probs = jax.nn.softmax(logits, axis=-1)
            rw, re = jax.lax.top_k(probs, TOP_K)
            if TOP_K > 1:
                rw = rw / jnp.maximum(rw.sum(-1, keepdims=True), 1e-12)
            rw = rw.astype(tokens.dtype)
            combine = jnp.zeros((N, E), tokens.dtype).at[jnp.arange(N)[:, None], re].set(rw)
            out = tokens
            for e in range(E):
                h = jax.nn.gelu(tokens @ w1[e] + b1[e], approximate=False)
                y = h @ w2[e] + b2[e]
                out = out + combine[:, e:e + 1] * y
            return out
        key = jax.random.key(seed)
        ks = jax.random.split(key, 4)
        scale = 1.0 / np.sqrt(D).astype(np.float32)
        return {'input_embeddings': jax.random.normal(ks[0], (B, S, D), jnp.float32), 'router_w': jax.random.normal(ks[1], (NUM_EXPERTS, D), jnp.float32) * scale, 'w1': jax.random.normal(ks[2], (NUM_EXPERTS, D, D), jnp.float32) * scale, 'b1': jnp.zeros((NUM_EXPERTS, D), jnp.float32), 'w2': jax.random.normal(ks[3], (NUM_EXPERTS, D, D), jnp.float32) * scale, 'b2': jnp.zeros((NUM_EXPERTS, D), jnp.float32)}
    _L1_ffn_all = _L1_ffn_setup()
    _L1_ffn_in = {k: v for k, v in _L1_ffn_all.items() if k in ('router_w', 'w1', 'b1', 'w2', 'b2')}
    del _L1_ffn_all
    return {'x': x, 'src': src, 'dst': dst, 'edge_type_8': edge_type_8, 'edge_weight': edge_weight, 'L0_gnn_Wp': _L0_gnn_in['Wp'], 'L0_gnn_bp': _L0_gnn_in['bp'], 'L0_gnn_W1': _L0_gnn_in['W1'], 'L0_gnn_b1': _L0_gnn_in['b1'], 'L0_gnn_W2': _L0_gnn_in['W2'], 'L0_gnn_b2': _L0_gnn_in['b2'], 'L0_ffn_gate_w': _L0_ffn_in['gate_w'], 'L0_ffn_gate_b': _L0_ffn_in['gate_b'], 'L0_ffn_W1': _L0_ffn_in['W1'], 'L0_ffn_b1': _L0_ffn_in['b1'], 'L0_ffn_W2': _L0_ffn_in['W2'], 'L0_ffn_b2': _L0_ffn_in['b2'], 'L1_gnn_weight': _L1_gnn_in['weight'], 'L1_ffn_router_w': _L1_ffn_in['router_w'], 'L1_ffn_w1': _L1_ffn_in['w1'], 'L1_ffn_b1': _L1_ffn_in['b1'], 'L1_ffn_w2': _L1_ffn_in['w2'], 'L1_ffn_b2': _L1_ffn_in['b2']}

def reference(x, src, dst, edge_type_8, edge_weight, L0_gnn_Wp, L0_gnn_bp, L0_gnn_W1, L0_gnn_b1, L0_gnn_W2, L0_gnn_b2, L0_ffn_gate_w, L0_ffn_gate_b, L0_ffn_W1, L0_ffn_b1, L0_ffn_W2, L0_ffn_b2, L1_gnn_weight, L1_ffn_router_w, L1_ffn_w1, L1_ffn_b1, L1_ffn_w2, L1_ffn_b2):
    import jax
    import jax.numpy as jnp

    def _L0_gnn_ref(x, edge_index, Wp, bp, W1, b1, W2, b2):
        import jax, jax.numpy as jnp
        import numpy as np
        N = 6250
        NEG_SLOPE = 0.1

        def gcn_conv(x, edge_index, W, b):
            src, dst = (edge_index[0], edge_index[1])
            loops = jnp.arange(N, dtype=src.dtype)
            row = jnp.concatenate([src, loops])
            col = jnp.concatenate([dst, loops])
            deg = jax.ops.segment_sum(jnp.ones(row.shape, x.dtype), col, num_segments=N)
            dis = jnp.where(deg > 0, jax.lax.rsqrt(deg), 0.0)
            norm = dis[row] * dis[col]
            h = x @ W
            msgs = h[row] * norm[:, None]
            out = jax.ops.segment_sum(msgs, col, num_segments=N)
            return out + b
        h = x @ Wp + bp
        h = h + gcn_conv(h, edge_index, W1, b1)
        h = h + gcn_conv(h, edge_index, W2, b2)
        return jax.nn.leaky_relu(h, NEG_SLOPE)

    def _L0_ffn_ref(x, gate_w, gate_b, W1, b1, W2, b2):
        import jax, jax.numpy as jnp
        import numpy as np
        B, T, D, H, E = (16, 512, 256, 512, 8)
        Bb, Tt, Dd = x.shape
        Ee = gate_w.shape[1]
        xf = x.reshape(-1, Dd)
        N = xf.shape[0]
        logits = xf @ gate_w + gate_b
        probs = jax.nn.softmax(logits, axis=-1)
        top2_vals, top2_idx = jax.lax.top_k(probs, 2)
        cw = jnp.zeros((N, Ee), dtype=xf.dtype).at[jnp.arange(N)[:, None], top2_idx].add(top2_vals)

        def step(acc, params):
            w1, bb1, w2, bb2, we = params
            h = jax.nn.gelu(xf @ w1 + bb1, approximate=False)
            y = h @ w2 + bb2
            return (acc + we[:, None] * y, None)
        out, _ = jax.lax.scan(step, jnp.zeros_like(xf), (W1, b1, W2, b2, cw.T))
        return out.reshape(Bb, Tt, Dd)

    def _L1_gnn_ref(h, norm, weight, edge_src, edge_dst, edge_type):
        import jax, jax.numpy as jnp
        import numpy as np
        N_NODES = 5000
        N_EDGES = 80000
        IN_FEAT = 256
        OUT_FEAT = 256
        NUM_RELS = 8
        transformed = jnp.einsum('ni,rio->rno', h, weight)
        msg = transformed[edge_type, edge_src] * norm[:, None]
        agg = jax.ops.segment_sum(msg, edge_dst, num_segments=h.shape[0])
        return jax.nn.relu(agg)

    def _L1_ffn_ref(input_embeddings, router_w, w1, b1, w2, b2):
        import jax, jax.numpy as jnp
        import numpy as np
        NUM_EXPERTS = 8
        TOP_K = 2
        B, S, D = (8, 1024, 256)

        def _moe(tokens, router_w, w1, b1, w2, b2):
            N = tokens.shape[0]
            E = router_w.shape[0]
            logits = tokens.astype(jnp.float32) @ router_w.astype(jnp.float32).T
            probs = jax.nn.softmax(logits, axis=-1)
            rw, re = jax.lax.top_k(probs, TOP_K)
            if TOP_K > 1:
                rw = rw / jnp.maximum(rw.sum(-1, keepdims=True), 1e-12)
            rw = rw.astype(tokens.dtype)
            combine = jnp.zeros((N, E), tokens.dtype).at[jnp.arange(N)[:, None], re].set(rw)
            out = tokens
            for e in range(E):
                h = jax.nn.gelu(tokens @ w1[e] + b1[e], approximate=False)
                y = h @ w2[e] + b2[e]
                out = out + combine[:, e:e + 1] * y
            return out
        b, s, d = input_embeddings.shape
        tokens = input_embeddings.reshape(b * s, d)
        return _moe(tokens, router_w, w1, b1, w2, b2).reshape(b, s, d)
    edge_index = jnp.stack([src, dst])
    x = x + _L0_gnn_ref(_layernorm(x, axis=-1), edge_index, L0_gnn_Wp, L0_gnn_bp, L0_gnn_W1, L0_gnn_b1, L0_gnn_W2, L0_gnn_b2)
    x = x + _L0_ffn_ref(_layernorm(x, axis=-1)[None], L0_ffn_gate_w, L0_ffn_gate_b, L0_ffn_W1, L0_ffn_b1, L0_ffn_W2, L0_ffn_b2)[0]
    x = x + _L1_gnn_ref(_layernorm(x, axis=-1), edge_weight, L1_gnn_weight, src, dst, edge_type_8)
    x = x + _L1_ffn_ref(_layernorm(x, axis=-1)[None], L1_ffn_router_w, L1_ffn_w1, L1_ffn_b1, L1_ffn_w2, L1_ffn_b2)[0]
    return x

_drawn_inputs = setup_inputs


def setup_inputs(seed=0):
    import zlib

    import numpy as np

    out = dict(_drawn_inputs(seed))
    spreads = {'L0_ffn_gate_b': (0.0, 0.32),
     'L0_ffn_b1': (0.0, 0.63),
     'L0_ffn_b2': (0.0, 0.1),
     'L1_ffn_b1': (0.0, 0.54),
     'L1_ffn_b2': (0.0, 0.379)}
    factors = {}
    for name, (base, spread) in spreads.items():
        noise = np.random.default_rng([zlib.crc32(name.encode()), seed]).standard_normal(out[name].shape)
        drawn = base * np.exp(spread * noise) if base else spread * noise
        out[name] = jnp.asarray(drawn.astype(out[name].dtype))
    for name, factor in factors.items():
        out[name] = (out[name] * factor).astype(out[name].dtype)
    return out
```

```python
from contextlib import ExitStack

import concourse.bass as bass
from concourse import mybir

F32 = mybir.dt.float32
BF16 = mybir.dt.bfloat16
I32 = mybir.dt.int32
U32 = mybir.dt.uint32
ALU = mybir.AluOpType
ACT = mybir.ActivationFunctionType
AX_X = mybir.AxisListType.X

P = 128
EPS = 1e-5
NEG_SLOPE = 0.1
SENTINEL = 8191
RING = 8
TPU = 2


def gnn_ffn_kernel(nc, a, out):
    N, D = a["x"].shape
    E = a["src"].shape[0]
    NX = a["L0_ffn_gate_w"].shape[1]
    NB = -(-N // P)
    NPAD = NB * P
    LAST = N - (NB - 1) * P
    KD = D // P
    UE = TPU * P
    NU = -(-E // UE)
    GROUPS = -(-NU // RING)
    NUP = GROUPS * RING
    UC = -(-(NUP + 1) // P)
    NCOL = UC * P * TPU
    ND = a["L1_gnn_weight"].shape[0]
    assert NUP + 1 <= UC * P and NB < 64 and NX == 8
    SLOTS = RING * TPU

    x = a["x"]
    ctx = ExitStack()
    with ctx:
        def sb(name, shape, dt=F32):
            return ctx.enter_context(nc.sbuf_tensor(name, shape, dt))

        def sem(name):
            return ctx.enter_context(nc.semaphore(name))

        def dram(name, shape):
            return nc.dram_tensor(name, shape, F32, kind="Internal").ap()

        x_pad = dram("x_pad", (NPAD, D))
        h0_d = dram("h0_d", (NPAD, D))
        h1_d = dram("h1_d", (NPAD, D))
        x2_d = dram("x2_d", (NPAD, D))
        t1_d = dram("t1_d", (NPAD, D))
        t2_d = dram("t2_d", (NPAD, D))
        t3_d = dram("t3_d", (NPAD * ND, D))
        t3_rows = t3_d.rearrange("(n r) d -> n (r d)", r=ND)

        ident = sb("ident", [P, P])
        iota = sb("iota", [P, P])
        iota_i = sb("iota_i", [P, P], I32)
        iota8 = sb("iota8", [P, NX])
        block_off = sb("block_off", [P, 64])
        ones = sb("ones", [P, 1])
        params = sb("params", [1, 4, 64], I32)
        dis = sb("dis", [P, NB])
        src_idx = sb("src_idx", [P, NCOL], I32)
        rel_idx = sb("rel_idx", [P, NCOL], I32)
        dst_t = sb("dst_t", [P, NCOL])
        w_t = sb("w_t", [P, NCOL])
        w_gcn = sb("w_gcn", [P, 3, KD, D])
        b_gcn = sb("b_gcn", [P, 3, D])
        gate = sb("gate", [P, 2, KD, NX])
        gate_b = sb("gate_b", [P, NX])
        w_rel = sb("w_rel", [P, KD, ND, D])
        F0 = a["L0_ffn_W1"].shape[2]
        F1 = a["L1_ffn_w1"].shape[2]
        KF0, KF1 = F0 // P, F1 // P
        moe0 = sb("moe0", [P, NX * (KD * F0 + KF0 * D + F0)])
        moe1 = moe0[:, 0:NX * (KD * F1 + KF1 * D + F1)]
        b2_sb = sb("b2_sb", [NX, 2, D])

        def moe_views(t, kf, f):
            n1, n2 = NX * KD * f, NX * kf * D
            return (t[:, 0:n1].rearrange("p (k e f) -> p k e f", k=KD, e=NX),
                    t[:, n1:n1 + n2].rearrange("p (k e d) -> p k e d", k=kf, e=NX),
                    t[:, n1 + n2:n1 + n2 + NX * f].rearrange("p (e f) -> p e f", e=NX))

        moe0_w1, moe0_w2, moe0_b1 = moe_views(moe0, KF0, F0)
        moe1_w1, moe1_w2, moe1_b1 = moe_views(moe1, KF1, F1)

        ring = sb("ring", [P, SLOTS, D])
        idx_now = sb("idx_now", [P, SLOTS], I32)
        onehot = sb("onehot", [P, TPU, P])
        ids = sb("ids", [P, P])

        h_in = sb("h_in", [P, 2, D])
        x_in = sb("x_in", [P, 2, D])
        s_sum = sb("s_sum", [P, D])
        s_tr = sb("s_tr", [P, KD, P])
        t_a = sb("t_a", [P, D])
        t_b = sb("t_b", [P, D])
        x_mid = sb("x_mid", [P, 2, D])
        l_mid = sb("l_mid", [P, D])
        l_tr = sb("l_tr", [P, KD, P])
        l2 = sb("l2", [P, D])
        l2_tr = sb("l2_tr", [P, KD, P])
        rel_out = sb("rel_out", [P, ND, D])
        acc = sb("acc", [P, D])
        hid = sb("hid", [P, 2, F0])
        gel = hid
        hid_tr = sb("hid_tr", [P, 2, KF0, P])
        stat = sb("stat", [P, 6])
        mv = sb("mv", [P, 2])
        ve = sb("ve", [P, 1])
        sd = sb("sd", [P, 1])
        rs = sb("rs", [P, 4])
        lg = sb("lg", [P, NX])
        nmx = sb("nmx", [P, 2])
        ex = sb("ex", [P, NX])
        exs = sb("exs", [P, 4])
        pr = sb("pr", [P, NX])
        top = sb("top", [P, 8])
        topi = sb("topi", [P, 8], U32)
        topf = sb("topf", [P, 8])
        cws = sb("cws", [P, 2, NX])
        cw = sb("cw", [P, NX])
        cw_tr = sb("cw_tr", [NX, P])

        raw = [moe0[:, n * UC * UE:(n + 1) * UC * UE].rearrange("p (c j) -> p c j", c=UC) for n in range(9)]
        x_all = moe0[:, 0:NB * D].rearrange("p (b d) -> p b d", b=NB)

        ps = [ctx.enter_context(nc.psum_tensor(f"ps{n}", [P, 512], F32)) for n in range(8)]

        arena_at = [NB * D]

        def early(shape, dt=F32):
            n = 1
            for d in shape[1:]:
                n *= d
            words = n if dt != BF16 else -(-n // 2)
            t = moe0[:, arena_at[0]:arena_at[0] + words]
            arena_at[0] += words
            if dt != F32:
                t = t.bitcast(dt)
            t = t[:, 0:n]
            if len(shape) == 3:
                t = t.rearrange("p (a b) -> p a b", a=shape[1])
            if len(shape) == 4:
                t = t.rearrange("p (a b c) -> p a b c", a=shape[1], b=shape[2])
            return t

        raw_i = [r.bitcast(I32) for r in raw]
        dst_r, dstn_r, src_r, typ_r = raw_i[0:4]
        w_r = raw[4]
        dst_f, dstn_f, src_f, typ_f = raw[5:9]
        dst_i = early([P, NCOL], I32)
        src_t = early([P, NCOL])
        hilo_i = early([P, NCOL], I32)
        lo_b = early([P, NCOL], BF16)
        hi_b = early([P, NCOL], BF16)
        iota_b = sb("iota_b", [P, P], BF16)
        oh_lo = early([P, 2, 8, P], BF16)
        oh_hi = early([P, 2, 8, NB], BF16)
        deg = sb("deg", [P, NB])
        deg_s = sb("deg_s", [P, 3, NB])
        tmin = sb("tmin", [P, UC])
        tmax = sb("tmax", [P, UC])
        nmin = sb("nmin", [P, UC])
        before = sb("before", [P, 64, UC])
        cnt = sb("cnt", [P, 64])
        row = sb("row", [1, 8, 64])

        s_fill, s_load, s_const, s_cf, s_raw = sem("fill"), sem("edges_in"), sem("consts"), sem("floats"), sem("w_in")
        s_etr, s_cnt, s_cps, s_oh, s_deg, s_taken = (sem("edge_tr"), sem("counts"), sem("count_sums"),
                                                    sem("deg_onehot"), sem("deg_sum"), sem("tables_taken"))
        s_dv, s_ds, s_misc = sem("deg_ready"), sem("deg_root"), sem("weights_in")
        FULL = (UC - 1) * P * UE
        rest_rows = (E - FULL) // UE
        rest = E - FULL - rest_rows * UE

        with nc.Block() as block:
            @block.sync
            def _(sp):
                sp.wait_ge(s_fill, 1)
                n = 0
                for name, dst, shift in (("dst", dst_r, 0), ("dst", dstn_r, 1), ("src", src_r, 0),
                                         ("edge_type_8", typ_r, 0), ("edge_weight", w_r, 0)):
                    flat = a[name]
                    sp.dma_start(dst[:, 0:UC - 1, :], flat[shift * UE:shift * UE + FULL].rearrange(
                        "(c p j) -> p c j", p=P, j=UE)).then_inc(s_load, 16)
                    at = shift * UE + FULL
                    rows = rest_rows - shift
                    sp.dma_start(dst[0:rows, UC - 1, :], flat[at:at + rows * UE].rearrange(
                        "(p j) -> p j", j=UE)).then_inc(s_load, 16)
                    n += 2
                    if rest:
                        sp.dma_start(dst[rows:rows + 1, UC - 1, 0:rest], flat[at + rows * UE:E].rearrange(
                            "(p j) -> p j", p=1)).then_inc(s_load, 16)
                        n += 1
                sp.wait_ge(s_load, 16 * n)
                sp.sem_inc(s_raw, 1)

            @block.gpsimd
            def _(pool):
                for r, v in ((dst_r, SENTINEL), (dstn_r, SENTINEL), (src_r, 0), (typ_r, 0)):
                    pool.memset(r[:, UC - 1, :], v)
                pool.memset(w_r[:, UC - 1, :], 0.0)
                pool.drain().then_inc(s_fill, 1)
                pool.memset(ident[:, :], 0.0)
                pool.memset(ones[:, :], 1.0)
                pool.iota(iota_i[:, :], pattern=[[1, P]], base=0, channel_multiplier=0)
                pool.drain()
                pool.affine_select(out=ident[:, :], in_=ident[:, :], compare_op=ALU.not_equal, fill=1.0, base=0,
                                   pattern=[[-1, P]], channel_multiplier=1)
                pool.tensor_copy(iota[:, :], iota_i[:, :])
                pool.tensor_copy(iota_b[:, :], iota_i[:, :])
                pool.tensor_copy(iota8[:, :], iota_i[:, 0:NX])
                pool.tensor_scalar(block_off[:, :], iota_i[:, 0:64], float(P), None, ALU.mult)
                pool.drain().then_inc(s_const, 1)

            @block.scalar
            def _(act):
                for m, w in enumerate(("L0_gnn_Wp", "L0_gnn_W1", "L0_gnn_W2")):
                    act.dma_start(w_gcn[:, m, :, :], a[w].rearrange("(k p) n -> p k n", p=P)).then_inc(s_misc, 16)
                for m, w in enumerate(("L0_gnn_bp", "L0_gnn_b1", "L0_gnn_b2")):
                    act.dma_start(b_gcn[:, m, :], a[w].partition_broadcast(P)).then_inc(s_misc, 16)
                act.dma_start(gate[:, 0, :, :], a["L0_ffn_gate_w"].rearrange("(k p) e -> p k e", p=P)).then_inc(s_misc, 16)
                for k in range(KD):
                    for e in range(NX):
                        act.dma_start(gate[:, 1, k, e:e + 1], a["L1_ffn_router_w"][e:e + 1, k * P:(k + 1) * P]
                                      .rearrange("e p -> p e")).then_inc(s_misc, 16)
                act.dma_start(gate_b[:, :], a["L0_ffn_gate_b"].partition_broadcast(P)).then_inc(s_misc, 16)
                act.dma_start(b2_sb[:, 0, :], a["L0_ffn_b2"]).then_inc(s_misc, 16)
                act.dma_start(b2_sb[:, 1, :], a["L1_ffn_b2"]).then_inc(s_misc, 16)
                for r in range(ND):
                    act.dma_start(w_rel[:, :, r, :], a["L1_gnn_weight"][r].rearrange("(k p) n -> p k n", p=P)).then_inc(s_misc, 16)
                act.wait_ge(s_dv, 1)
                act.activation(deg_s[:, 0, :], deg[:, :], ACT.Sqrt).then_inc(s_ds, 1)
                act.wait_ge(s_misc, 16 * (3 + 3 + 1 + KD * NX + 1 + 2 + ND))

            @block.vector
            def _(dve):
                dve.memset(deg[:, :], 0.0)
                dve.wait_ge(s_raw, 1)
                for f, r in ((dst_f, dst_r), (dstn_f, dstn_r), (src_f, src_r), (typ_f, typ_r)):
                    dve.tensor_copy(f, r)
                dve.drain().then_inc(s_cf, 1)
                dve.tensor_reduce(tmin[:, :], dst_f, AX_X, ALU.min)
                dve.tensor_reduce(tmax[:, :], dst_f, AX_X, ALU.max)
                dve.tensor_reduce(nmin[:, :], dstn_f, AX_X, ALU.min)
                dve.wait_ge(s_const, 1)
                dve.tensor_scalar(before[:, :, 0], block_off[:, :], float(P), None, ALU.add)
                dve.drain()
                dve.tensor_copy(cnt[:, :], before[:, :, 0])
                dve.drain()
                dve.tensor_tensor(before[:, :, :], tmin[:, None, :].broadcast_to([P, 64, UC]),
                                  cnt[:, :, None].broadcast_to([P, 64, UC]), ALU.is_lt)
                dve.drain()
                dve.tensor_tensor(before[:, 63, :], tmax[:, :], nmin[:, :], ALU.is_gt)
                dve.drain()
                dve.tensor_reduce(cnt[:, :], before[:, :, :], AX_X, ALU.add).then_inc(s_cnt, 1)
                def by_tile(t):
                    return t[:, :].rearrange("p (u j) -> p j u", j=TPU)

                dve.wait_ge(s_etr, 4)
                for j in range(TPU):
                    dve.tensor_copy(by_tile(dst_t)[:, j, :], ps[j][:, :])
                    dve.tensor_copy(by_tile(src_idx)[:, j, :], ps[2 + j][:, :])
                    dve.tensor_copy(by_tile(w_t)[:, j, :], ps[6 + j][:, :])
                    dve.tensor_scalar(by_tile(src_t)[:, j, :], ps[2 + j][:, :], float(ND), None, ALU.mult)
                dve.drain()
                for j in range(TPU):
                    dve.tensor_tensor(by_tile(rel_idx)[:, j, :], by_tile(src_t)[:, j, :], ps[4 + j][:, :], ALU.add)
                dve.drain().then_inc(s_taken, 1)
                dve.tensor_copy(dst_i[:, :], dst_t[:, :])
                dve.drain()
                dve.tensor_scalar(hilo_i[:, :], dst_i[:, :], P - 1, None, ALU.bitwise_and)
                dve.drain()
                dve.tensor_copy(lo_b[:, :], hilo_i[:, :])
                dve.drain()
                dve.tensor_scalar(hilo_i[:, :], dst_i[:, :], P.bit_length() - 1, None, ALU.arith_shift_right)
                dve.drain()
                dve.tensor_copy(hi_b[:, :], hilo_i[:, :])
                dve.drain()
                dve.wait_ge(s_cps, 1)
                r = row[:, :, :]
                A, C, NN, FL, T, T2 = 0, 1, 2, 3, 4, 5
                def done():
                    dve.drain()
                dve.tensor_scalar(r[:, T, :], ps[0][0:1, 0:64], 1.0, None, ALU.max)
                dve.tensor_scalar(r[:, FL, 0:1], ps[0][0:1, 63:64], 1.0, None, ALU.min)
                done()
                dve.memset(r[:, T, NB - 1:64], float(NUP))
                dve.memset(r[:, C, 0:1], 0.0)
                done()
                dve.tensor_scalar(r[:, C, 1:64], r[:, T, 0:63], -1.0, None, ALU.add)
                done()
                dve.tensor_tensor(r[:, NN, :], r[:, T, :], r[:, C, :], ALU.subtract)
                dve.tensor_scalar(r[:, T2, :], block_off[0:1, 0:64], float(NUP) / P, None, ALU.mult)
                done()
                dve.tensor_tensor(r[:, T, :], r[:, T2, :], r[:, C, :], ALU.subtract)
                done()
                dve.tensor_scalar(r[:, T2, :], r[:, NN, :], -1.0, float(NUP + 1), ALU.mult, ALU.add)
                done()
                dve.scalar_tensor_tensor(out=r[:, A, :], in0=r[:, T, :], scalar=r[:, FL, 0:1], in1=r[:, C, :],
                                         op0=ALU.mult, op1=ALU.add)
                dve.scalar_tensor_tensor(out=r[:, 6, :], in0=r[:, T2, :], scalar=r[:, FL, 0:1], in1=r[:, NN, :],
                                         op0=ALU.mult, op1=ALU.add)
                dve.tensor_scalar(r[:, 7, 0:1], r[:, FL, 0:1], -1.0, 1.0, ALU.mult, ALU.add)
                done()
                dve.tensor_copy(params[:, 0, :], r[:, A, :])
                dve.tensor_copy(params[:, 1, :], r[:, 6, :])
                dve.tensor_scalar(params[:, 2, :], r[:, C, :], r[:, 7, 0:1], None, ALU.mult)
                dve.tensor_scalar(params[:, 3, :], r[:, FL, 0:1].broadcast_to([1, 64]), float(GROUPS * NB + 1 - GROUPS),
                                  float(GROUPS), ALU.mult, ALU.add)
                done()
                with dve.Fori(0, NUP * TPU // 16) as g:
                    for h in range(2):
                        cols = bass.ds(g * 16 + h * 8, 8)
                        dve.tensor_tensor(oh_lo[:, h, :, :], iota_b[:, None, :].broadcast_to([P, 8, P]),
                                          lo_b[:, cols][:, :, None].broadcast_to([P, 8, P]), ALU.is_equal)
                        dve.tensor_tensor(oh_hi[:, h, :, :], iota_b[:, None, 0:NB].broadcast_to([P, 8, NB]),
                                          hi_b[:, cols][:, :, None].broadcast_to([P, 8, NB]), ALU.is_equal)
                        dve.drain().then_inc(s_oh, 1)
                    for h in range(2):
                        dve.wait_ge(s_deg, g * 2 + h + 1)
                        dve.tensor_tensor(deg[:, :], deg[:, :], ps[6 + h][:, 0:NB], ALU.add)
                        dve.drain()
                dve.tensor_scalar(deg[:, :], deg[:, :], 1.0, None, ALU.add)
                dve.drain().then_inc(s_dv, 1)
                dve.wait_ge(s_ds, 1)
                dve.reciprocal(deg_s[:, 1, :], deg_s[:, 0, :])
                dve.drain()
                dve.tensor_tensor(deg_s[:, 2, :], deg_s[:, 1, :], deg_s[:, 1, :], ALU.mult)
                dve.drain()
                dve.tensor_tensor(deg_s[:, 2, :], deg_s[:, 2, :], deg[:, :], ALU.mult)
                dve.drain()
                dve.tensor_scalar(deg_s[:, 2, :], deg_s[:, 2, :], -0.5, 1.5, ALU.mult, ALU.add)
                dve.drain()
                dve.tensor_tensor(dis[:, :], deg_s[:, 1, :], deg_s[:, 2, :], ALU.mult)
                dve.drain()

            @block.tensor
            def _(pe):
                pe.wait_ge(s_const, 1)
                pe.wait_ge(s_cf, 1)
                for n, t in enumerate((dst_f, src_f, typ_f, w_r)):
                    for j in range(TPU):
                        for c in range(UC):
                            m = pe.transpose(ps[2 * n + j][:, c * P:(c + 1) * P], t[:, c, j * P:(j + 1) * P], ident[:, :])
                    m.then_inc(s_etr, 1)
                pe.wait_ge(s_cnt, 1)
                pe.wait_ge(s_taken, 1)
                pe.matmul(ps[0][0:1, 0:64], ones[:, :], cnt[:, :], start=True, stop=True).then_inc(s_cps, 1)
                with pe.Fori(0, NUP * TPU // 16) as g:
                    for h in range(2):
                        pe.wait_ge(s_oh, g * 2 + h + 1)
                        for t in range(8):
                            m = pe.matmul(ps[6 + h][:, 0:NB], oh_lo[:, h, t, :], oh_hi[:, h, t, :], start=(t == 0), stop=(t == 7))
                        m.then_inc(s_deg, 1)

        mv_all = sb("mv_all", [P, NB, 2])
        stats = sb("stats", [P, 2, 6])
        rstd_all = sb("rstd_all", [P, 3, NB])
        arena_at[0] = NB * D
        ln = early([P, 2, D])
        ln_tr = early([P, 2, KD, P])
        h_out = sb("h_out", [P, 2, D])
        t_out = sb("t_out", [P, 2, D])
        s_xz, s_x, s_xs, s_ve, s_sd = sem("x_padded"), sem("x_in"), sem("x_saved"), sem("var_all"), sem("std_all")
        s_ln, s_lt, s_lc, s_h, s_ho = sem("ln"), sem("ln_tr"), sem("ln_tr_sb"), sem("h0"), sem("h0_sb")
        s_hd = [sem(f"h0_saved{n}") for n in range(2)]

        def pairs(eng, count, body):
            with eng.Fori(0, count // 2) as g:
                body(g * 2, 0, g)
                body(g * 2 + 1, 1, g)
            body(count - 1, 0, count // 2)

        with nc.Block() as block:
            @block.sync
            def _(sp):
                sp.dma_start(x_all[:, 0:NB - 1, :], x[0:(NB - 1) * P, :].rearrange("(b p) d -> p b d", p=P)).then_inc(s_x, 16)
                sp.wait_ge(s_xz, 1)
                sp.dma_start(x_all[0:LAST, NB - 1, :], x[(NB - 1) * P:N, :]).then_inc(s_x, 16)
                sp.wait_ge(s_x, 32)
                sp.dma_start(x_pad.rearrange("(b p) d -> p b d", p=P), x_all).then_inc(s_xs, 16)

                def save(b, par, g):
                    sp.wait_ge(s_ho, b + 1)
                    sp.dma_start(h0_d[bass.ds(b * P, P), :], h_out[:, par, :]).then_inc(s_hd[par], 16)
                    sp.dma_start(t1_d[bass.ds(b * P, P), :], t_out[:, par, :]).then_inc(s_hd[par], 16)
                pairs(sp, NB, save)
                sp.wait_ge(s_xs, 16)
                sp.wait_ge(s_hd[0], 32 * (NB // 2 + 1))
                sp.wait_ge(s_hd[1], 32 * (NB // 2))

            @block.gpsimd
            def _(pool):
                pool.memset(x_all[:, NB - 1, :], 0.0)
                pool.drain().then_inc(s_xz, 1)

            @block.scalar
            def _(act):
                act.wait_ge(s_ve, 1)
                act.activation(rstd_all[:, 1, :], rstd_all[:, 0, :], ACT.Sqrt).then_inc(s_sd, 1)

                def copy(b, par, g):
                    act.wait_ge(s_lt, b + 1)
                    act.copy(ln_tr[:, par, :, :].rearrange("p k n -> p (k n)"), ps[par][:, 0:D]).then_inc(s_lc, 1)
                pairs(act, NB, copy)

            @block.tensor
            def _(pe):
                def product(b, par, g):
                    pe.wait_ge(s_lc, b + 1)
                    for k in range(KD):
                        m = pe.matmul(ps[2 + par][:, 0:D], ln_tr[:, par, k, :], w_gcn[:, 0, k, :], start=(k == 0), stop=(k == KD - 1))
                    m.then_inc(s_h, 1)

                def turn(b, par, g):
                    pe.wait_ge(s_ln, b + 1)
                    for k in range(KD):
                        m = pe.transpose(ps[par][:, k * P:(k + 1) * P], ln[:, par, k * P:(k + 1) * P], ident[:, :])
                    m.then_inc(s_lt, 1)

                def step(b, par, g):
                    turn(b, par, g)
                    product(b, par, g)
                pairs(pe, NB, step)

            @block.vector
            def _(dve):
                dve.wait_ge(s_x, 32)
                dve.wait_ge(s_xz, 1)
                with dve.Fori(0, NB) as b:
                    dve.bn_stats(stats[:, 0, :], x_all[:, bass.ds(b, 1), :].rearrange("p b d -> p (b d)"))
                    dve.drain()
                    dve.bn_aggr(stats[:, 1, 0:2], stats[:, 0, :])
                    dve.drain()
                    dve.tensor_copy(mv_all[:, bass.ds(b, 1), :].rearrange("p b d -> p (b d)"), stats[:, 1, 0:2])
                    dve.drain()
                dve.tensor_scalar(rstd_all[:, 0, :], mv_all[:, :, 1], EPS, None, ALU.add)
                dve.drain().then_inc(s_ve, 1)
                dve.wait_ge(s_sd, 1)
                dve.reciprocal(rstd_all[:, 2, :], rstd_all[:, 1, :])
                dve.drain()
                dve.tensor_tensor(rstd_all[:, 1, :], rstd_all[:, 2, :], rstd_all[:, 2, :], ALU.mult)
                dve.drain()
                dve.tensor_tensor(rstd_all[:, 1, :], rstd_all[:, 1, :], rstd_all[:, 0, :], ALU.mult)
                dve.drain()
                dve.tensor_scalar(rstd_all[:, 1, :], rstd_all[:, 1, :], -0.5, 1.5, ALU.mult, ALU.add)
                dve.drain()
                dve.tensor_tensor(rstd_all[:, 0, :], rstd_all[:, 1, :], rstd_all[:, 2, :], ALU.mult)
                dve.drain()

                def norm(b, par):
                    dve.tensor_scalar(ln[:, par, :], x_all[:, bass.ds(b, 1), :].rearrange("p b d -> p (b d)"),
                                      mv_all[:, bass.ds(b, 1), 0], rstd_all[:, 0, bass.ds(b, 1)],
                                      ALU.subtract, ALU.mult).then_inc(s_ln, 1)

                def step(b, par, g):
                    if not (isinstance(b, int) and b == NB - 1):
                        dve.wait_ge(s_h, b + 0) if isinstance(b, int) and b else None
                        norm(b + 1, 1 - par)
                    dve.wait_ge(s_h, b + 1)
                    if par == 0:
                        dve.wait_ge(s_hd[0], g * 32) if not isinstance(g, int) else dve.wait_ge(s_hd[0], g * 32)
                    else:
                        dve.wait_ge(s_hd[1], g * 32)
                    dve.tensor_tensor(h_out[:, par, :], ps[2 + par][:, 0:D], b_gcn[:, 0, :], ALU.add)
                    dve.drain()
                    dve.tensor_scalar(t_out[:, par, :], h_out[:, par, :], dis[:, bass.ds(b, 1)], None, ALU.mult)
                    dve.drain().then_inc(s_ho, 1)
                norm(0, 0)
                pairs(dve, NB, step)

        def flat(t):
            return t.rearrange("p a b -> p (a b)")

        def sweep(lag, body):
            def at(i):
                return lambda l: 0 <= i - l < NB

            def run(eng):
                for i in range(lag):
                    body(i, at(i))
                with eng.Fori(lag, NB - 1) as i:
                    body(i, lambda l: True)
                for i in range(NB - 1, NB + lag):
                    body(i, at(i))
            return run

        slot_sems = [sem(f"ring_slot{k}") for k in range(SLOTS)]

        class Sums:

            def __init__(self, name, before):
                self.before = before
                self.free = sem(f"{name}_units_free")
                self.slot = slot_sems
                self.idx = sem(f"{name}_indices")
                self.idx_free = sem(f"{name}_indices_free")
                self.landed = sem(f"{name}_tiles_landed")
                self.oh = sem(f"{name}_onehot")
                self.mm = sem(f"{name}_products")

            def gather(self, pool, table, cols):
                pool.sem_inc(self.free, RING)
                groups = pool.value_load(params[0:1, 3, 0:1], min_val=GROUPS, max_val=GROUPS * NB + 1)
                pool.sem_inc(self.idx_free, 2)
                half = RING // 2
                with pool.Fori(0, groups) as i:
                    for h in range(2):
                        pool.wait_ge(self.idx_free, i * 2 + (h + 1))
                        pool.nop(nofuse=True)
                        n = half * TPU
                        pool.tensor_copy(idx_now[:, h * n:(h + 1) * n],
                                         cols[:, bass.ds((i % GROUPS) * SLOTS + h * n, n)]).then_inc(self.idx, 1)
                        pool.wait_ge(self.idx, i * 2 + (h + 1))
                        pool.nop(nofuse=True)
                        for u in range(h * half, (h + 1) * half):
                            pool.wait_ge(self.free, i * RING + (u + 1))
                            pool.nop(nofuse=True)
                            for k in range(u * TPU, (u + 1) * TPU):
                                pool.indirect_dma_start(ring[:, k, :], None, table,
                                                        bass.IndirectOffsetOnAxis(idx_now[:, k:k + 1], 0)).then_inc(self.slot[k], 16)

            def land(self, sp):
                groups = sp.value_load(params[0:1, 3, 0:1], min_val=GROUPS, max_val=GROUPS * NB + 1)
                with sp.Fori(0, groups) as i:
                    for k in range(SLOTS):
                        sp.wait_ge(self.slot[k], (i + groups * self.before + 1) * 16)
                        sp.sem_inc(self.landed, 1)
                        if (k + 1) % (SLOTS // 2) == 0:
                            sp.sem_inc(self.idx_free, 1)

            def load(self, eng, b, with_column=False):
                first = eng.value_load(params[0:1, 0, bass.ds(b, 1)], min_val=0, max_val=NUP * NB)
                count = eng.value_load(params[0:1, 1, bass.ds(b, 1)], min_val=1, max_val=NUP + 1)
                if not with_column:
                    return first, count
                return first, count, eng.value_load(params[0:1, 2, bass.ds(b, 1)], min_val=0, max_val=NUP - 1)

            def each(self, eng, count, unit):
                unit(0, True)
                with eng.If(count > 1):
                    with eng.Fori(1, count) as k:
                        unit(k, False)
                eng.nop(nofuse=True)

            def onehots(self, dve, b, weights):
                first, count, column = self.load(dve, b, True)
                dve.tensor_scalar(ids[:, :], iota[:, :], block_off[:, bass.ds(b, 1)], None, ALU.add)
                dve.drain()

                def unit(k, is_first):
                    unit_at = nc.s_assert_within(column + k, 0, NUP, skip_runtime_bounds_check_because="a block's units end at NUP")
                    for j in range(TPU):
                        dve.wait_ge(self.mm, (first + b + k) * 2 + (j + 1))
                        if j == 1 and not is_first:
                            dve.sem_inc(self.free, 1)
                        col = bass.ds(unit_at * 2 + j, 1)
                        if weights:
                            m = dve.tensor_scalar(onehot[:, j, :], ids[:, :], dst_t[:, col], w_t[:, col], ALU.is_equal, ALU.mult)
                        else:
                            m = dve.tensor_scalar(onehot[:, j, :], ids[:, :], dst_t[:, col], None, ALU.is_equal)
                        m.then_inc(self.oh, 1)
                self.each(dve, count, unit)
                dve.wait_ge(self.mm, (first + b + count) * 2 + 2)

            def products(self, pe, b):
                first, count = self.load(pe, b)

                def unit(k, is_first):
                    for j in range(TPU):
                        pe.wait_ge(self.landed, (first + k) * 2 + (j + 1))
                        pe.wait_ge(self.oh, (first + b + k) * 2 + (j + 1))
                        at = ((first + k) % RING) * TPU + j
                        pe.matmul(ps[0][:, 0:D], onehot[:, j, :], ring[:, bass.ds(at, 1), :].rearrange("p a d -> p (a d)"),
                                  start=(is_first and j == 0), stop=True, skip_group_check=True).then_inc(self.mm, 1)
                self.each(pe, count, unit)

        class Norm:

            def __init__(self, name):
                self.ve, self.sd = sem(f"{name}_var"), sem(f"{name}_std")

            def on_dve(self, dve, b, src, dst):
                dve.bn_stats(stat[:, :], src)
                dve.drain()
                dve.bn_aggr(mv[:, :], stat[:, :])
                dve.drain()
                dve.tensor_scalar(ve[:, :], mv[:, 1:2], EPS, None, ALU.add)
                dve.drain().then_inc(self.ve, 1)
                dve.wait_ge(self.sd, b + 1)
                dve.reciprocal(rs[:, 0:1], sd[:, :])
                dve.drain()
                dve.scalar_tensor_tensor(out=rs[:, 1:2], in0=rs[:, 0:1], scalar=rs[:, 0:1], in1=ve[:, :], op0=ALU.mult, op1=ALU.mult)
                dve.drain()
                dve.tensor_scalar(rs[:, 2:3], rs[:, 1:2], -0.5, 1.5, ALU.mult, ALU.add)
                dve.drain()
                dve.tensor_tensor(rs[:, 3:4], rs[:, 2:3], rs[:, 0:1], ALU.mult)
                dve.drain()
                return dve.tensor_scalar(dst, src, mv[:, 0:1], rs[:, 3:4], ALU.subtract, ALU.mult)

            def on_act(self, act, b):
                act.wait_ge(self.ve, b + 1)
                act.activation(sd[:, :], ve[:, :], ACT.Sqrt).then_inc(self.sd, 1)

        class Conv:

            def __init__(self, name, m):
                self.m = m
                self.sum, self.tr, self.trc, self.out = (sem(f"{name}_sum"), sem(f"{name}_sum_tr"),
                                                         sem(f"{name}_sum_tr_sb"), sem(f"{name}_conv"))

            def sum_dve(self, dve, b):
                dve.scalar_tensor_tensor(out=s_sum[:, :], in0=flat(h_in[:, bass.ds(b % 2, 1), :]), scalar=dis[:, bass.ds(b, 1)],
                                         in1=ps[0][:, 0:D], op0=ALU.mult, op1=ALU.add).then_inc(self.sum, 1)

            def on_pe(self, pe, b):
                pe.wait_ge(self.sum, b + 1)
                for k in range(KD):
                    m = pe.transpose(ps[1][:, k * P:(k + 1) * P], s_sum[:, k * P:(k + 1) * P], ident[:, :])
                m.then_inc(self.tr, 1)
                pe.wait_ge(self.trc, b + 1)
                for k in range(KD):
                    m = pe.matmul(ps[2][:, 0:D], s_tr[:, k, :], w_gcn[:, self.m, k, :], start=(k == 0), stop=(k == KD - 1))
                m.then_inc(self.out, 1)

            def on_act(self, act, b):
                act.wait_ge(self.tr, b + 1)
                act.copy(flat(s_tr[:, :, :]), ps[1][:, 0:D]).then_inc(self.trc, 1)

            def out_dve(self, dve, b):
                dve.wait_ge(self.out, b + 1)
                dve.scalar_tensor_tensor(out=t_a[:, :], in0=ps[2][:, 0:D], scalar=dis[:, bass.ds(b, 1)],
                                         in1=flat(h_in[:, bass.ds(b % 2, 1), :]), op0=ALU.mult, op1=ALU.add)
                dve.drain()
                dve.tensor_tensor(t_b[:, :], t_a[:, :], b_gcn[:, self.m, :], ALU.add)
                dve.drain()

        class Load:

            def __init__(self, name, src, dst):
                self.src, self.dst, self.s = src, dst, sem(f"{name}_loaded")

            def issue(self, act, b):
                if not isinstance(b, int) or b > 0:
                    act.wait_ge(self.s, b * 16)
                act.dma_start(flat(self.dst[:, bass.ds(b % 2, 1), :]), self.src[bass.ds(b * P, P), :]).then_inc(self.s, 16)

            def wait(self, eng, b):
                eng.wait_ge(self.s, b * 16 + 16)

        sums1, conv1 = Sums("g1", 0), Conv("g1", 1)
        load_h0 = Load("h0", h0_d, h_in)
        s_h1, s_h1d, s_moe0, s_moe1 = sem("h1"), sem("h1_saved"), sem("moe0_in"), sem("moe1_in")
        with nc.Block() as block:
            @block.sync
            def _(sp):
                for e in range(NX):
                    sp.dma_start(moe0_w1[:, :, e, :], a["L0_ffn_W1"][e].rearrange("(k p) n -> p k n", p=P)).then_inc(s_moe0, 16)
                    sp.dma_start(moe0_w2[:, :, e, :], a["L0_ffn_W2"][e].rearrange("(k p) n -> p k n", p=P)).then_inc(s_moe0, 16)
                    sp.dma_start(moe0_b1[:, e, :], a["L0_ffn_b1"][e].partition_broadcast(P)).then_inc(s_moe0, 16)
                sums1.land(sp)
                sp.wait_ge(s_moe0, 16 * 3 * NX)

            @block.gpsimd
            def _(pool):
                sums1.gather(pool, t1_d, src_idx[:, :])

            @block.scalar
            def _(act):
                load_h0.issue(act, 0)

                def body(i, live):
                    if live(1):
                        conv1.on_act(act, i - 1)
                        act.wait_ge(s_h1, i)
                        act.dma_start(h1_d[bass.ds((i - 1) * P, P), :], h_out[:, 0, :]).then_inc(s_h1d, 16)
                        act.dma_start(t2_d[bass.ds((i - 1) * P, P), :], t_out[:, 0, :]).then_inc(s_h1d, 16)
                    if live(-1):
                        load_h0.issue(act, i + 1)
                sweep(1, body)(act)
                act.wait_ge(s_h1d, 32 * NB)

            @block.tensor
            def _(pe):
                def body(i, live):
                    if live(1):
                        conv1.on_pe(pe, i - 1)
                    if live(0):
                        sums1.products(pe, i)
                sweep(1, body)(pe)

            @block.vector
            def _(dve):
                dve.sem_inc(sums1.mm, 2)

                def body(i, live):
                    if live(1):
                        dve.wait_ge(s_h1d, (i - 1) * 32)
                        conv1.out_dve(dve, i - 1)
                        dve.tensor_copy(h_out[:, 0, :], t_b[:, :])
                        dve.tensor_scalar(t_out[:, 0, :], t_b[:, :], dis[:, bass.ds(i - 1, 1)], None, ALU.mult)
                        dve.drain().then_inc(s_h1, 1)
                    if live(0):
                        sums1.onehots(dve, i, False)
                        load_h0.wait(dve, i)
                        conv1.sum_dve(dve, i)
                sweep(1, body)(dve)

        class Moe:
            def __init__(self, name, which, f, w1, w2, b1):
                self.which, self.f, self.kf, self.w1, self.w2, self.b1 = which, f, f // P, w1, w2, b1
                self.lt, self.ltc = sem(f"{name}_tokens_tr"), sem(f"{name}_tokens_tr_sb")
                self.lg, self.lgs, self.ex = sem(f"{name}_logits"), sem(f"{name}_logits_sb"), sem(f"{name}_exps")
                self.cw, self.cwt, self.cwtc = sem(f"{name}_weights"), sem(f"{name}_weights_tr"), sem(f"{name}_weights_tr_sb")
                self.b2 = sem(f"{name}_biases2")
                self.H, self.hid, self.gel, self.T = sem(f"{name}_H"), sem(f"{name}_hid"), sem(f"{name}_gelu"), sem(f"{name}_T")
                self.hT, self.Y, self.acc = sem(f"{name}_T_sb"), sem(f"{name}_Y"), sem(f"{name}_acc")

            def router_pe(self, pe, b):
                for k in range(KD):
                    m = pe.transpose(ps[1][:, k * P:(k + 1) * P], l_mid[:, k * P:(k + 1) * P], ident[:, :])
                m.then_inc(self.lt, 1)
                pe.wait_ge(self.ltc, b + 1)
                for k in range(KD):
                    m = pe.matmul(ps[2][:, D:D + NX], l_tr[:, k, :], gate[:, self.which, k, :], start=(k == 0), stop=(k == KD - 1))
                m.then_inc(self.lg, 1)

            def router_act(self, act, b):
                act.wait_ge(self.lt, b + 1)
                act.copy(flat(l_tr[:, :, :]), ps[1][:, 0:D]).then_inc(self.ltc, 1)
                act.wait_ge(self.lgs, b + 1)
                act.activation(ex[:, :], lg[:, :], ACT.Exp, bias=nmx[:, 0:1], accum_out=exs[:, 0:1])
                act.drain().then_inc(self.ex, 1)

            def router_dve(self, dve, b):
                dve.wait_ge(self.lg, b + 1)
                if self.which == 0:
                    dve.tensor_tensor(lg[:, :], ps[2][:, D:D + NX], gate_b[:, :], ALU.add)
                else:
                    dve.tensor_copy(lg[:, :], ps[2][:, D:D + NX])
                dve.drain()
                dve.tensor_reduce(nmx[:, 1:2], lg[:, :], AX_X, ALU.max)
                dve.drain()
                dve.tensor_scalar(nmx[:, 0:1], nmx[:, 1:2], -1.0, None, ALU.mult)
                dve.drain().then_inc(self.lgs, 1)
                dve.wait_ge(self.ex, b + 1)
                dve.reciprocal(exs[:, 1:2], exs[:, 0:1])
                dve.drain()
                dve.tensor_scalar(pr[:, :], ex[:, :], exs[:, 1:2], None, ALU.mult)
                dve.drain()
                dve.max(top[:, :], pr[:, :])
                dve.drain()
                dve.max_index(topi[:, :], top[:, :], pr[:, :])
                dve.drain()
                dve.tensor_copy(topf[:, :], topi[:, :])
                if self.which == 1:
                    dve.tensor_tensor(exs[:, 2:3], top[:, 0:1], top[:, 1:2], ALU.add)
                    dve.drain()
                    dve.tensor_scalar(exs[:, 3:4], exs[:, 2:3], 1e-12, None, ALU.max)
                    dve.drain()
                    dve.reciprocal(exs[:, 2:3], exs[:, 3:4])
                dve.drain()
                for n in range(2):
                    dve.tensor_scalar(cws[:, n, :], iota8[:, :], topf[:, n:n + 1], top[:, n:n + 1], ALU.is_equal, ALU.mult)
                dve.drain()
                if self.which == 1:
                    dve.tensor_tensor(pr[:, :], cws[:, 0, :], cws[:, 1, :], ALU.add)
                    dve.drain()
                    dve.tensor_scalar(cw[:, :], pr[:, :], exs[:, 2:3], None, ALU.mult)
                else:
                    dve.tensor_tensor(cw[:, :], cws[:, 0, :], cws[:, 1, :], ALU.add)
                dve.drain().then_inc(self.cw, 1)

            def experts_pe(self, pe, b, h_free):
                f = self.f

                def H(e):
                    if e >= 2:
                        pe.wait_ge(self.hid, b * NX + (e - 1))
                    for k in range(KD):
                        m = pe.matmul(ps[3 + e % 2][:, 0:f], l_tr[:, k, :], self.w1[:, k, e, :], start=(k == 0), stop=(k == KD - 1))
                    m.then_inc(self.H, 1)

                def T(e):
                    pe.wait_ge(self.gel, b * NX + (e + 1))
                    for c in range(self.kf):
                        m = pe.transpose(ps[5][:, c * P:(c + 1) * P], gel[:, e % 2, c * P:(c + 1) * P], ident[:, :])
                    m.then_inc(self.T, 1)

                def Y(e):
                    pe.wait_ge(self.hT, b * NX + (e + 1))
                    if e >= 2:
                        pe.wait_ge(self.acc, b * NX + (e - 1))
                    for c in range(self.kf):
                        m = pe.matmul(ps[6 + e % 2][:, 0:D], hid_tr[:, e % 2, c, :], self.w2[:, c, e, :], start=(c == 0), stop=(c == self.kf - 1))
                    m.then_inc(self.Y, 1)

                h_free()
                H(0)
                H(1)
                pe.wait_ge(self.cw, b + 1)
                pe.transpose(ps[2][0:NX, 384:384 + P], cw[:, :], ident[:, :]).then_inc(self.cwt, 1)
                pe.wait_ge(self.cwtc, b + 1)
                pe.matmul(ps[2][:, 0:D], cw_tr[:, :], b2_sb[:, self.which, :], start=True, stop=True).then_inc(self.b2, 1)
                T(0)
                for e in range(1, NX):
                    if e + 1 < NX:
                        H(e + 1)
                    Y(e - 1)
                    T(e)
                Y(NX - 1)

            def experts_act(self, act, b):
                f = self.f

                def gelu(e):
                    act.wait_ge(self.hid, b * NX + (e + 1))
                    act.activation(gel[:, e % 2, 0:f], hid[:, e % 2, 0:f], ACT.Gelu).then_inc(self.gel, 1)

                def copy(e):
                    act.wait_ge(self.T, b * NX + (e + 1))
                    act.copy(flat(hid_tr[:, e % 2, 0:self.kf, :]), ps[5][:, 0:f]).then_inc(self.hT, 1)
                gelu(0)
                act.wait_ge(self.cwt, b + 1)
                act.copy(cw_tr[:, :], ps[2][0:NX, 384:384 + P]).then_inc(self.cwtc, 1)
                for e in range(NX):
                    if e + 1 < NX:
                        gelu(e + 1)
                    copy(e)

            def experts_dve(self, dve, b, first):
                f = self.f

                def hid_(e):
                    dve.wait_ge(self.H, b * NX + (e + 1))
                    if e >= 2:
                        dve.wait_ge(self.gel, b * NX + (e - 1))
                    dve.tensor_tensor(hid[:, e % 2, 0:f], ps[3 + e % 2][:, 0:f], self.b1[:, e, :], ALU.add).then_inc(self.hid, 1)

                def acc_(e):
                    dve.wait_ge(self.Y, b * NX + (e + 1))
                    dve.scalar_tensor_tensor(out=acc[:, :], in0=ps[6 + e % 2][:, 0:D], scalar=cw[:, e:e + 1], in1=acc[:, :],
                                             op0=ALU.mult, op1=ALU.add)
                    dve.drain().then_inc(self.acc, 1)
                hid_(0)
                hid_(1)
                dve.wait_ge(self.b2, b + 1)
                first()
                for e in range(1, NX):
                    if e + 1 < NX:
                        hid_(e + 1)
                    acc_(e - 1)
                acc_(NX - 1)

        sums2, conv2 = Sums("g2", 1), Conv("g2", 2)
        load_h1, load_x = Load("h1", h1_d, h_in), Load("x", x_pad, x_in)
        norm1, norm2 = Norm("n1"), Norm("n2")
        moe_a = Moe("m0", 0, F0, moe0_w1, moe0_w2, moe0_b1)
        s_l1, s_x2, s_x2d, s_l2 = sem("l1"), sem("x2"), sem("x2_saved"), sem("l2")
        s_l2t, s_l2c, s_rel, s_relc, s_reld = sem("l2_tr"), sem("l2_tr_sb"), sem("rel"), sem("rel_sb"), sem("rel_saved")
        RP = ND * D // 512
        with nc.Block() as block:
            @block.sync
            def _(sp):
                sums2.land(sp)

            @block.gpsimd
            def _(pool):
                sums2.gather(pool, t2_d, src_idx[:, :])

            @block.scalar
            def _(act):
                load_h1.issue(act, 0)
                load_x.issue(act, 0)

                def body(i, live):
                    if live(1):
                        conv2.on_act(act, i - 1)
                        norm1.on_act(act, i - 1)
                    if live(-1):
                        load_h1.issue(act, i + 1)
                        load_x.issue(act, i + 1)
                    if live(1):
                        moe_a.router_act(act, i - 1)
                    if live(2):
                        b = i - 2
                        act.wait_ge(s_l2t, b + 1)
                        act.copy(flat(l2_tr[:, :, :]), ps[1][:, D:2 * D]).then_inc(s_l2c, 1)
                        act.wait_ge(s_reld, b * 16)
                        for n in range(RP):
                            act.wait_ge(s_rel, b * RP + (n + 1))
                            act.copy(flat(rel_out[:, :, :])[:, n * 512:(n + 1) * 512], ps[3 + n % 2][:, :]).then_inc(s_relc, 1)
                        act.wait_ge(s_relc, (b + 1) * RP)
                        act.dma_start(t3_rows[bass.ds(b * P, P), :], flat(rel_out[:, :, :])).then_inc(s_reld, 16)
                    if live(1):
                        moe_a.experts_act(act, i - 1)
                        norm2.on_act(act, i - 1)
                        act.dma_start(x2_d[bass.ds((i - 1) * P, P), :], acc[:, :]).then_inc(s_x2d, 16)
                sweep(2, body)(act)
                act.wait_ge(s_reld, 16 * NB)
                act.wait_ge(s_x2d, 16 * NB)

            @block.tensor
            def _(pe):
                def body(i, live):
                    if live(1):
                        conv2.on_pe(pe, i - 1)
                    if live(0):
                        sums2.products(pe, i)
                    if live(1):
                        pe.wait_ge(s_l1, i)
                        moe_a.router_pe(pe, i - 1)
                    if live(2):
                        b = i - 2
                        pe.wait_ge(s_l2, b + 1)
                        for k in range(KD):
                            m = pe.transpose(ps[1][:, D + k * P:D + (k + 1) * P], l2[:, k * P:(k + 1) * P], ident[:, :])
                        m.then_inc(s_l2t, 1)
                        pe.wait_ge(s_l2c, b + 1)
                        for n in range(RP):
                            if n >= 2:
                                pe.wait_ge(s_relc, b * RP + (n - 1))
                            for k in range(KD):
                                m = pe.matmul(ps[3 + n % 2][:, :], l2_tr[:, k, :],
                                              w_rel[:, k, :, :].rearrange("p r d -> p (r d)")[:, n * 512:(n + 1) * 512],
                                              start=(k == 0), stop=(k == KD - 1))
                            m.then_inc(s_rel, 1)
                    if live(1):
                        def h_free():
                            if live(2):
                                pe.wait_ge(s_relc, (i - 1) * RP)
                        moe_a.experts_pe(pe, i - 1, h_free)
                sweep(2, body)(pe)

            @block.vector
            def _(dve):
                dve.sem_inc(sums2.mm, 2)

                def body(i, live):
                    if live(1):
                        conv2.out_dve(dve, i - 1)
                        dve.scalar_tensor_tensor(out=t_a[:, :], in0=t_b[:, :], scalar=NEG_SLOPE, in1=t_b[:, :],
                                                 op0=ALU.mult, op1=ALU.max)
                        dve.drain()
                        load_x.wait(dve, i - 1)
                        dve.tensor_tensor(x_mid[:, 0, :], t_a[:, :], flat(x_in[:, bass.ds((i - 1) % 2, 1), :]), ALU.add)
                        dve.drain()
                        norm1.on_dve(dve, i - 1, x_mid[:, 0, :], l_mid[:, :])
                        dve.drain().then_inc(s_l1, 1)
                    if live(0):
                        sums2.onehots(dve, i, False)
                        load_h1.wait(dve, i)
                        conv2.sum_dve(dve, i)
                    if live(1):
                        moe_a.router_dve(dve, i - 1)
                        dve.wait_ge(s_x2d, (i - 1) * 16)

                        def first():
                            dve.tensor_tensor(acc[:, :], ps[2][:, 0:D], x_mid[:, 0, :], ALU.add)
                            dve.drain()
                        moe_a.experts_dve(dve, i - 1, first)
                        norm2.on_dve(dve, i - 1, acc[:, :], l2[:, :])
                        dve.drain().then_inc(s_l2, 1)
                sweep(2, body)(dve)

        sums3 = Sums("g3", 2)
        load_x2 = Load("x2", x2_d, x_in)
        norm3 = Norm("n3")
        moe_b = Moe("m1", 1, F1, moe1_w1, moe1_w2, moe1_b1)
        s_x3, s_l3, s_y, s_yd = sem("x3"), sem("l3"), sem("y"), sem("y_saved")
        with nc.Block() as block:
            @block.sync
            def _(sp):
                for e in range(NX):
                    sp.dma_start(moe1_w1[:, :, e, :], a["L1_ffn_w1"][e].rearrange("(k p) n -> p k n", p=P)).then_inc(s_moe1, 16)
                    sp.dma_start(moe1_w2[:, :, e, :], a["L1_ffn_w2"][e].rearrange("(k p) n -> p k n", p=P)).then_inc(s_moe1, 16)
                    sp.dma_start(moe1_b1[:, e, :], a["L1_ffn_b1"][e].partition_broadcast(P)).then_inc(s_moe1, 16)
                sums3.land(sp)
                sp.wait_ge(s_moe1, 16 * 3 * NX)

            @block.gpsimd
            def _(pool):
                sums3.gather(pool, t3_d, rel_idx[:, :])

            @block.scalar
            def _(act):
                load_x2.issue(act, 0)

                def body(i, live):
                    if live(1):
                        norm3.on_act(act, i - 1)
                    if live(-1):
                        load_x2.issue(act, i + 1)
                    if live(1):
                        moe_b.router_act(act, i - 1)
                        moe_b.experts_act(act, i - 1)
                        act.wait_ge(s_y, i)
                        if isinstance(i, int) and i - 1 == NB - 1:
                            act.dma_start(out[(NB - 1) * P:N, :], acc[0:LAST, :]).then_inc(s_yd, 16)
                        else:
                            act.dma_start(out[bass.ds((i - 1) * P, P), :], acc[:, :]).then_inc(s_yd, 16)
                sweep(1, body)(act)
                act.wait_ge(s_yd, 16 * NB)

            @block.tensor
            def _(pe):
                pe.wait_ge(s_moe1, 16 * 3 * NX)

                def body(i, live):
                    if live(0):
                        if not isinstance(i, int) or i > 0:
                            pe.wait_ge(s_x3, i)
                        sums3.products(pe, i)
                    if live(1):
                        pe.wait_ge(s_l3, i)
                        moe_b.router_pe(pe, i - 1)
                        moe_b.experts_pe(pe, i - 1, lambda: None)
                sweep(1, body)(pe)

            @block.vector
            def _(dve):
                dve.sem_inc(sums3.mm, 2)

                dve.wait_ge(s_moe1, 16 * 3 * NX)

                def body(i, live):
                    if live(1):
                        x3 = flat(x_mid[:, bass.ds((i - 1) % 2, 1), :])
                        norm3.on_dve(dve, i - 1, x3, l_mid[:, :])
                        dve.drain().then_inc(s_l3, 1)
                    if live(0):
                        sums3.onehots(dve, i, True)
                        load_x2.wait(dve, i)
                        dve.scalar_tensor_tensor(out=flat(x_mid[:, bass.ds(i % 2, 1), :]), in0=ps[0][:, 0:D], scalar=0.0,
                                                 in1=flat(x_in[:, bass.ds(i % 2, 1), :]), op0=ALU.max, op1=ALU.add)
                        dve.drain().then_inc(s_x3, 1)
                    if live(1):
                        moe_b.router_dve(dve, i - 1)
                        dve.wait_ge(s_yd, (i - 1) * 16)

                        def first():
                            dve.tensor_tensor(t_a[:, :], ps[2][:, 0:D], l_mid[:, :], ALU.add)
                            dve.drain()
                            dve.tensor_tensor(acc[:, :], t_a[:, :], x3, ALU.add)
                            dve.drain()
                        moe_b.experts_dve(dve, i - 1, first)
                        dve.drain().then_inc(s_y, 1)
                sweep(1, body)(dve)


_INS = ["x", "src", "dst", "edge_type_8", "edge_weight",
        "L0_gnn_Wp", "L0_gnn_bp", "L0_gnn_W1", "L0_gnn_b1", "L0_gnn_W2", "L0_gnn_b2",
        "L0_ffn_gate_w", "L0_ffn_gate_b", "L0_ffn_W1", "L0_ffn_b1", "L0_ffn_W2", "L0_ffn_b2",
        "L1_gnn_weight", "L1_ffn_router_w", "L1_ffn_w1", "L1_ffn_b1", "L1_ffn_w2", "L1_ffn_b2"]


def kernel(**inputs):
    import numpy as _np
    import concourse.bacc as _bacc
    from concourse import mybir as _mybir
    from concourse.bass_utils import run_bass_kernel_spmd as _run

    nc = _bacc.Bacc("TRN2", target_bir_lowering=False, num_devices=1)
    arrays, args = {}, {}
    for name in _INS:
        v = _np.ascontiguousarray(inputs[name])
        arrays[f"in_{name}_dram"] = v
        args[name] = nc.dram_tensor(f"in_{name}_dram", v.shape, _mybir.dt.from_np(v.dtype), kind="ExternalInput").ap()
    out = nc.dram_tensor("out_0_dram", inputs["x"].shape, _mybir.dt.float32, kind="ExternalOutput").ap()
    gnn_ffn_kernel(nc, args, out)
    r = _run(nc, [arrays], core_ids=[0])
    return r.results[0]["out_0_dram"]
```
